# Optimizing a Trainium2 kernel written in Bass

```python
import numpy as np
import jax
import jax.numpy as jnp

def _softmax(x, axis=-1):
    return jax.nn.softmax(x, axis=axis)

def _gelu(x):
    return jax.nn.gelu(x, approximate=True)

def _silu(x):
    return jax.nn.silu(x)

def _sigmoid(x):
    return jax.nn.sigmoid(x)

def _layernorm(x, axis=-1, eps=1e-05):
    m = jnp.mean(x, axis=axis, keepdims=True)
    v = jnp.var(x, axis=axis, keepdims=True)
    return (x - m) / jnp.sqrt(v + eps)

def _scatter_add(tgt, idx, src, axis=0):
    return tgt.at[idx].add(src)

def _segment_sum(src, seg, n):
    return jax.ops.segment_sum(src, seg, n)
kernel_name = 'mk_macaron_d1_jaxref_r8_55c88b'

def setup_inputs(seed: int=0):
    np.random.seed(seed)
    _w = jnp.asarray

    def _L0_attn_setup():
        import jax, jax.numpy as jnp
        import numpy as np
        B, L, D = (4, 1024, 128)
        N = D
        EPS = 1e-05

        def _ssm_scan(a, x):

            def combine(c1, c2):
                a1, b1 = c1
                a2, b2 = c2
                return (a1 * a2, a2 * b1 + b2)
            _, h = jax.lax.associative_scan(combine, (a, x), axis=1)
            return h
        key = jax.random.key(seed)
        ks = jax.random.split(key, 9)
        s = 1.0 / np.sqrt(D)
        return {'x': jax.random.normal(ks[0], (B, L, D), dtype=jnp.float32), 'norm_w': jnp.ones((D,), dtype=jnp.float32), 'A_w': jax.random.uniform(ks[1], (N, D), minval=-s, maxval=s), 'A_b': jax.random.uniform(ks[2], (N,), minval=-s, maxval=s), 'B_w': jax.random.uniform(ks[3], (N, D), minval=-s, maxval=s), 'C_w': jax.random.uniform(ks[4], (N, D), minval=-s, maxval=s), 'D_w': jax.random.uniform(ks[5], (N, D), minval=-s, maxval=s), 'out_w': jax.random.uniform(ks[6], (D, N), minval=-s, maxval=s), 'out_b': jax.random.uniform(ks[7], (D,), minval=-s, maxval=s)}
    _L0_attn_in = _L0_attn_setup()

    def _L0_ffn_setup():
        import jax, jax.numpy as jnp
        import numpy as np
        DIM = 128
        HIDDEN = 384
        SCALE = 1.0 / 127.0

        def _dequant(w_int, dtype):
            return w_int.astype(dtype) * jnp.asarray(SCALE, dtype)
        key = jax.random.key(seed)
        k_x, k_g, k_u, k_d = jax.random.split(key, 4)
        x = jax.random.normal(k_x, (4, 256, DIM), dtype=jnp.float32)
        w_gate = jax.random.randint(k_g, (HIDDEN, DIM), -127, 128, dtype=jnp.int32)
        w_up = jax.random.randint(k_u, (HIDDEN, DIM), -127, 128, dtype=jnp.int32)
        w_down = jax.random.randint(k_d, (DIM, HIDDEN), -127, 128, dtype=jnp.int32)
        return {'x': x, 'w_gate': w_gate, 'w_up': w_up, 'w_down': w_down}
    _L0_ffn_in = _L0_ffn_setup()
    _d = {'L0_attn_x': _L0_attn_in['x'], 'L0_attn_norm_w': _L0_attn_in['norm_w'], 'L0_attn_A_w': _L0_attn_in['A_w'], 'L0_attn_A_b': _L0_attn_in['A_b'], 'L0_attn_B_w': _L0_attn_in['B_w'], 'L0_attn_C_w': _L0_attn_in['C_w'], 'L0_attn_D_w': _L0_attn_in['D_w'], 'L0_attn_out_w': _L0_attn_in['out_w'], 'L0_attn_out_b': _L0_attn_in['out_b'], 'L0_ffn_w_gate': _L0_ffn_in['w_gate'], 'L0_ffn_w_up': _L0_ffn_in['w_up'], 'L0_ffn_w_down': _L0_ffn_in['w_down']}
    _x0 = _d['L0_attn_x']
    _d['L0_attn_x'] = jax.random.normal(jax.random.fold_in(jax.random.key(seed), 1), (2, 1024, 128), dtype=_x0.dtype)
    del _x0
    return _d

def reference(L0_attn_x, L0_attn_norm_w, L0_attn_A_w, L0_attn_A_b, L0_attn_B_w, L0_attn_C_w, L0_attn_D_w, L0_attn_out_w, L0_attn_out_b, L0_ffn_w_gate, L0_ffn_w_up, L0_ffn_w_down):

    def _L0_attn_ref(x, norm_w, A_w, A_b, B_w, C_w, D_w, out_w, out_b):
        import jax, jax.numpy as jnp
        import numpy as np
        B, L, D = (4, 1024, 128)
        N = D
        EPS = 1e-05

        def _ssm_scan(a, x):

            def combine(c1, c2):
                a1, b1 = c1
                a2, b2 = c2
                return (a1 * a2, a2 * b1 + b2)
            _, h = jax.lax.associative_scan(combine, (a, x), axis=1)
            return h
        residual = x
        norm = jnp.sqrt(jnp.mean(x * x, axis=-1, keepdims=True) + EPS)
        xn = x * (norm_w / norm)
        a = jax.nn.sigmoid(jnp.einsum('bld,nd->bln', xn, A_w) + A_b)
        b = jnp.einsum('bld,nd->bln', xn, B_w)
        c = jax.nn.sigmoid(jnp.einsum('bld,nd->bln', xn, C_w))
        d = jax.nn.sigmoid(jnp.einsum('bld,nd->bln', xn, D_w))
        h = c * _ssm_scan(a, d * b)
        y = jnp.einsum('bln,dn->bld', h, out_w) + out_b
        return y + residual

    def _L0_ffn_ref(x, w_gate, w_up, w_down):
        import jax, jax.numpy as jnp
        import numpy as np
        DIM = 128
        HIDDEN = 384
        SCALE = 1.0 / 127.0

        def _dequant(w_int, dtype):
            return w_int.astype(dtype) * jnp.asarray(SCALE, dtype)
        wg = _dequant(w_gate, x.dtype)
        wu = _dequant(w_up, x.dtype)
        wd = _dequant(w_down, x.dtype)
        gate = jnp.einsum('bsd,hd->bsh', x, wg)
        up = jnp.einsum('bsd,hd->bsh', x, wu)
        h = jax.nn.silu(gate) * up
        return jnp.einsum('bsh,dh->bsd', h, wd)
    x = L0_attn_x
    x = x + 0.5 * _L0_ffn_ref(_layernorm(x, axis=-1), L0_ffn_w_gate, L0_ffn_w_up, L0_ffn_w_down)
    x = x + _L0_attn_ref(_layernorm(x, axis=-1), L0_attn_norm_w, L0_attn_A_w, L0_attn_A_b, L0_attn_B_w, L0_attn_C_w, L0_attn_D_w, L0_attn_out_w, L0_attn_out_b)
    x = x + 0.5 * _L0_ffn_ref(_layernorm(x, axis=-1), L0_ffn_w_gate, L0_ffn_w_up, L0_ffn_w_down)
    return x

_drawn_inputs = setup_inputs


def setup_inputs(seed=0):
    import zlib

    import numpy as np

    out = dict(_drawn_inputs(seed))
    spreads = {'L0_attn_norm_w': (1.0, 0.6)}
    factors = {'L0_attn_A_w': 8.0,
     'L0_attn_A_b': 56.632,
     'L0_attn_B_w': 8.0,
     'L0_attn_C_w': 8.0,
     'L0_attn_D_w': 8.0,
     'L0_attn_out_w': 8.0,
     'L0_attn_out_b': 64.0}
    for name, (base, spread) in spreads.items():
        noise = np.random.default_rng([zlib.crc32(name.encode()), seed]).standard_normal(out[name].shape)
        drawn = base * np.exp(spread * noise) if base else spread * noise
        out[name] = jnp.asarray(drawn.astype(out[name].dtype))
    for name, factor in factors.items():
        out[name] = (out[name] * factor).astype(out[name].dtype)
    return out
```

```python
from contextlib import ExitStack

import concourse.bass as bass
from concourse import mybir

F32 = mybir.dt.float32
F32R = mybir.dt.float32r
I32 = mybir.dt.int32
ALU = mybir.AluOpType
ACT = mybir.ActivationFunctionType

P = 128
EPS = 1e-05
SCALE = 1.0 / 127.0
FFN1, SSM, FFN2 = 1, 2, 3

UNITS = [(FFN1, 0), (FFN1, 1), (FFN1, 2), (SSM, 0), (FFN1, 3), (SSM, 1), (SSM, 2), (FFN2, 0), (SSM, 3),
         (FFN2, 1), (FFN2, 2), (FFN2, 3)]
NU = len(UNITS)


def is_ssm(u):
    return UNITS[u][0] == SSM


def reader_of(u):
    layer, chunk = UNITS[u]
    return None if layer == FFN2 else UNITS.index((layer + 1, chunk))


def preps_in(slot):
    early = {0: -1, 1: -1, 2: 0, 4: 2}
    found = [u for u, s in early.items() if s == slot]
    if 0 <= slot - 2 < NU and reader_of(slot - 2) is not None:
        found.append(reader_of(slot - 2))
    return sorted(found)


def macaron_kernel(nc, x, norm_w, A_w, A_b, B_w, C_w, D_w, out_w, out_b, w_gate, w_up, w_down, out):
    B, L, D = x.shape
    H = w_gate.shape[0]
    J = H // P
    NC = 4
    T = B * L // NC
    R = T // P
    HALVES = NC // B
    assert D == P and H == J * P and T == 512 and A_w.shape == (P, P)

    def rows(ap, chunk):
        seq, half = chunk % B, chunk // B
        return ap[seq, half * T:(half + 1) * T, :].rearrange("(t p) d -> p t d", p=P)

    parts = [sum(1 if is_ssm(v) else J for v in range(u)) for u in range(NU + 1)]
    pairs = [2 + sum(2 if is_ssm(v) else J for v in range(u)) for u in range(NU + 1)]
    ffns = [sum(not is_ssm(v) for v in range(u)) for u in range(NU + 1)]

    with ExitStack() as ctx:
        def sb(name, shape, dt=F32):
            return ctx.enter_context(nc.sbuf_tensor(name, shape, dt))

        def ps(name):
            return ctx.enter_context(nc.psum_tensor(name, [P, 512], F32))

        def sem(name):
            return ctx.enter_context(nc.semaphore(name))

        x_in = sb("x_in", [P, NC, R, D])
        x_ffn = sb("x_ffn", [P, NC, R, D])
        x_plus = sb("x_plus", [P, NC, R, D])
        x_ssm = sb("x_ssm", [P, NC, R, D])
        x_out = sb("x_out", [P, NC, R, D])
        ident = sb("ident", [P, P])
        bn = sb("bn", [P, NU, R, 6])
        meanvar = sb("meanvar", [P, NU, R, 2])
        negmean = sb("negmean", [P, NU, R])
        pow_in = sb("pow_in", [P, NU, 2 * R])
        rstd = sb("rstd", [P, NU, 2 * R])
        rstd1 = sb("rstd1", [P, NC, R])
        negmr = sb("negmr", [P, NC, R])
        half_power = sb("half_power", [P, 2 * R])
        normed = sb("normed", [P, 4, R, D])
        xhi = sb("xhi", [P, 2, T], F32R)
        xlo = sb("xlo", [P, 2, T], F32R)
        act = sb("act", [P, 2, J, T])
        h = sb("h", [P, 2, J, T])
        hhi = sb("hhi", [P, 2, J, T], F32R)
        hlo = sb("hlo", [P, 2, J, T], F32R)
        tanh_d = sb("tanh_d", [P, 2, T])
        tanh_a = sb("tanh_a", [P, 2, T])
        tanh_c = sb("tanh_c", [P, 2, T])
        decay = sb("decay", [P, 2, T])
        drive = sb("drive", [P, 2, T])
        state = sb("state", [P, NC, T])
        closed = sb("closed", [P, 2, T])
        gu_int = sb("gu_int", [P, 2, J, P], I32)
        gu_raw = sb("gu_raw", [P, 2, J, P])
        gu_hi = sb("gu_hi", [P, 2, J, P], F32R)
        gu_lo = sb("gu_lo", [P, 2, J, P], F32R)
        down_int = sb("down_int", [P, J, P], I32)
        close_raw = sb("close_raw", [P, J + 1, P])
        close_hi = sb("close_hi", [P, J + 1, P], F32R)
        close_lo = sb("close_lo", [P, J + 1, P], F32R)
        proj_raw = sb("proj_raw", [P, 4, P])
        proj_scaled = sb("proj_scaled", [P, 4, P])
        proj_hi = sb("proj_hi", [P, 4, P], F32R)
        proj_lo = sb("proj_lo", [P, 4, P], F32R)
        vecs = sb("vecs", [P, 3])
        half_ab = sb("half_ab", [P, 1])
        warm = sb("warm", [P, 1])

        pair = [[ps("pair0a"), ps("pair0b")], [ps("pair1a"), ps("pair1b")]]
        turned = ps("turned")
        acc = ps("acc")
        back = ps("back")

        x_loaded = [sem(f"x_loaded{c}") for c in range(NC)]
        gu_loaded = sem("gu_loaded")
        down_loaded = sem("down_loaded")
        ssm_loaded = sem("ssm_loaded")
        vecs_loaded = sem("vecs_loaded")
        x_stored = sem("x_stored")
        ident_ready = sem("ident_ready")
        const_ready = sem("const_ready")
        vec_own = sem("vec_own")
        pool_own = sem("pool_own")
        gu_cast = sem("gu_cast")
        down_cast = sem("down_cast")
        weights_turned = sem("weights_turned")
        weights_hi = sem("weights_hi")
        scaled_ready = sem("scaled_ready")
        weights_lo = sem("weights_lo")
        stats_ready = sem("stats_ready")
        normed_ready = sem("normed_ready")
        plus_ready = sem("plus_ready")
        turned_ready = sem("turned_ready")
        xhi_ready = sem("xhi_ready")
        xlo_ready = sem("xlo_ready")
        gate_ready = sem("gate_ready")
        up_ready = sem("up_ready")
        silu_ready = sem("silu_ready")
        pair_done = sem("pair_done")
        proj_ready = sem("proj_ready")
        tanh_ready = sem("tanh_ready")
        gated_ready = sem("gated_ready")
        hhi_ready = sem("hhi_ready")
        hlo_ready = sem("hlo_ready")
        acc_ready = sem("acc_ready")
        closed_ready = sem("closed_ready")
        back_ready = sem("back_ready")
        rows_ready = sem("rows_ready")

        def source(u):
            layer, c = UNITS[u]
            return {FFN1: x_in, SSM: x_ffn, FFN2: x_ssm}[layer][:, c]

        block = ctx.enter_context(nc.Block())

        @block.sync
        def _(sp):
            sp.dma_start(x_in[:, 0], rows(x, 0)).then_inc(x_loaded[0], 16)
            sp.dma_start(gu_int[:, 1], w_up.rearrange("(j p) d -> p j d", p=P)).then_inc(gu_loaded, 16)
            sp.dma_start(x_in[:, 1], rows(x, 1)).then_inc(x_loaded[1], 16)
            sp.dma_start(close_raw[:, J], out_w).then_inc(ssm_loaded, 16)
            for n, w in enumerate((D_w, B_w, A_w, C_w)):
                sp.dma_start(proj_raw[:, n], w).then_inc(ssm_loaded, 16)
            for c in range(2, NC):
                sp.dma_start(x_in[:, c], rows(x, c)).then_inc(x_loaded[c], 16)
            for u in range(NU):
                layer, c = UNITS[u]
                if layer == FFN2:
                    sp.wait_ge(rows_ready, u + 1)
                    sp.dma_start(rows(out, c), x_out[:, c]).then_inc(x_stored, 16)
            sp.wait_ge(x_stored, 16 * NC)

        @block.gpsimd
        def _(pool):
            own = [0]

            def then_wait(ins):
                own[0] += 1
                ins.then_inc(pool_own, 1)
                pool.wait_ge(pool_own, own[0])

            then_wait(nc.gpsimd.memset(ident[:], 0.0))
            nc.gpsimd.affine_select(out=ident[:], in_=ident[:], compare_op=ALU.not_equal, fill=1.0, base=0,
                                    pattern=[[-1, P]], channel_multiplier=1).then_inc(ident_ready, 1)
            then_wait(nc.gpsimd.memset(half_power[:], -0.5))

            def prep(u):
                layer, c = UNITS[u]
                n = 2 * R if layer == SSM else R
                pool.wait_ge(stats_ready, u + 1)
                then_wait(nc.gpsimd.tensor_tensor(rstd[:, u, 0:n], pow_in[:, u, 0:n], half_power[:, 0:n], ALU.pow))
                if u >= 4:
                    pool.wait_ge(turned_ready, u - 3)
                for t in range(R):
                    s = R + t if layer == SSM else t
                    last = nc.gpsimd.tensor_scalar(normed[:, u % 4, t], source(u)[:, t], negmean[:, u, t:t + 1],
                                                   rstd[:, u, s:s + 1], ALU.add, ALU.mult)
                last.then_inc(normed_ready, 1)
                if layer == SSM:
                    nc.gpsimd.tensor_scalar(rstd1[:, c], rstd[:, u, 0:R], 1.0, 1.0, ALU.mult, ALU.add)
                    then_wait(nc.gpsimd.tensor_tensor(negmr[:, c], negmean[:, u], rstd[:, u, 0:R], ALU.mult))
                    for t in range(R):
                        last = nc.gpsimd.tensor_scalar(x_plus[:, c, t], source(u)[:, t], rstd1[:, c, t:t + 1],
                                                       negmr[:, c, t:t + 1], ALU.mult, ALU.add)
                    last.then_inc(plus_ready, 1)

            def low_part(u, j):
                pool.wait_ge(hhi_ready, parts[u] + j + 1)
                nc.gpsimd.tensor_tensor(hlo[:, u % 2, j], h[:, u % 2, j], hhi[:, u % 2, j].bitcast(F32),
                                        ALU.subtract).then_inc(hlo_ready, 1)

            for u in preps_in(-1):
                prep(u)
            for k in range(NU + 2):
                if k < NU and not is_ssm(k):
                    for j in range(J - 1):
                        low_part(k, j)
                for u in preps_in(k):
                    prep(u)
                if k < NU:
                    low_part(k, 0 if is_ssm(k) else J - 1)

        @block.scalar
        def _(sc):
            sc.dma_start(gu_int[:, 0], w_gate.rearrange("(j p) d -> p j d", p=P)).then_inc(gu_loaded, 16)
            sc.dma_start(down_int[:], w_down.rearrange("d (j h) -> d j h", h=P)).then_inc(down_loaded, 16)
            for n, v in enumerate((norm_w, A_b, out_b)):
                sc.dma_start(vecs[:, n:n + 1], v.rearrange("(p o) -> p o", o=1)).then_inc(vecs_loaded, 16)
            sc.wait_ge(const_ready, 1)
            nc.scalar.activation(warm[:], warm[:], ACT.Silu)
            sc.wait_ge(weights_turned, 1)
            for n in range(2):
                last = nc.scalar.activation(gu_hi[:, n].rearrange("p j h -> p (j h)"), pair[0][n][:, 0:H], ACT.Copy)
            last.then_inc(weights_hi, 1)

            def turn(u):
                sc.wait_ge(turned_ready, u + 1)
                nc.scalar.activation(xhi[:, u % 2], turned[:], ACT.Copy).then_inc(xhi_ready, 1)

            def high_part(u, j):
                if is_ssm(u):
                    sc.wait_ge(gated_ready, UNITS[u][1] + 1)
                else:
                    sc.wait_ge(pair_done, pairs[u] + j + 1)
                nc.scalar.activation(hhi[:, u % 2, j], h[:, u % 2, j], ACT.Copy).then_inc(hhi_ready, 1)

            def silu(u, j):
                g = pairs[u] + j
                sc.wait_ge(gate_ready, ffns[u] * J + j + 1)
                nc.scalar.activation(act[:, u % 2, j], pair[g % 2][0][:], ACT.Silu, scale=SCALE).then_inc(silu_ready, 1)

            def tanh(u, n):
                g, c = pairs[u], UNITS[u][1]
                bank = (pair[g % 2][0], pair[(g + 1) % 2][0], pair[(g + 1) % 2][1])[n]
                dst = (tanh_d, tanh_a, tanh_c)[n]
                sc.wait_ge(proj_ready, 4 * c + (1, 3, 4)[n])
                nc.scalar.activation(dst[:, c % 2], bank[:], ACT.Tanh, scale=0.5,
                                     bias=half_ab[:] if n == 1 else 0.0).then_inc(tanh_ready, 1)

            def close(u):
                sc.wait_ge(acc_ready, u + 1)
                if is_ssm(u):
                    nc.scalar.activation(closed[:, u % 2], acc[:], ACT.Identity, scale=0.25,
                                         bias=vecs[:, 2:3]).then_inc(closed_ready, 1)
                else:
                    nc.scalar.activation(closed[:, u % 2], acc[:], ACT.Copy,
                                         scale=0.5 * SCALE * SCALE).then_inc(closed_ready, 1)

            turn(0)
            sc.wait_ge(weights_turned, 2)
            nc.scalar.activation(close_hi[:].rearrange("p j h -> p (j h)"), pair[1][0][:], ACT.Copy).then_inc(weights_hi, 1)
            sc.wait_ge(scaled_ready, 1)
            nc.scalar.activation(proj_hi[:], proj_scaled[:], ACT.Copy).then_inc(weights_hi, 1)

            for k in range(NU + 2):
                if k < NU and is_ssm(k):
                    for n in range(3):
                        tanh(k, n)
                    if k + 1 < NU:
                        turn(k + 1)
                    if k:
                        close(k - 1)
                    high_part(k, 0)
                elif k < NU:
                    silu(k, 0)
                    silu(k, 1)
                    high_part(k, 0)
                    silu(k, 2)
                    high_part(k, 1)
                    if k + 1 < NU:
                        turn(k + 1)
                    high_part(k, 2)
                    if k:
                        close(k - 1)
                elif k == NU:
                    close(k - 1)

        @block.vector
        def _(ve):
            own = [0]

            def then_wait(ins):
                own[0] += 1
                ins.then_inc(vec_own, 1)
                ve.wait_ge(vec_own, own[0])

            def prep(u):
                layer, c = UNITS[u]
                if layer == FFN1:
                    ve.wait_ge(x_loaded[c], 16)
                else:
                    ve.wait_ge(rows_ready, UNITS.index((layer - 1, c)) + 1)
                for t in range(R):
                    last = nc.vector.bn_stats(bn[:, u, t], source(u)[:, t])
                then_wait(last)
                for t in range(R):
                    last = nc.vector.bn_aggr(meanvar[:, u, t], bn[:, u, t])
                then_wait(last)
                nc.vector.tensor_scalar(negmean[:, u], meanvar[:, u, :, 0], -1.0, None, ALU.mult)
                if layer == SSM:
                    nc.vector.tensor_scalar(pow_in[:, u, R:2 * R], meanvar[:, u, :, 1], 1.0 + EPS, EPS * EPS,
                                            ALU.mult, ALU.add)
                nc.vector.tensor_scalar(pow_in[:, u, 0:R], meanvar[:, u, :, 1], EPS, None,
                                        ALU.add).then_inc(stats_ready, 1)

            def turn(u):
                ve.wait_ge(turned_ready, u + 1)
                ve.wait_ge(xhi_ready, u + 1)
                nc.vector.tensor_tensor(xlo[:, u % 2], turned[:], xhi[:, u % 2].bitcast(F32),
                                        ALU.subtract).then_inc(xlo_ready, 1)

            def gate_times_up(u, j):
                ve.wait_ge(silu_ready, ffns[u] * J + j + 1)
                ve.wait_ge(up_ready, ffns[u] * J + j + 1)
                nc.vector.tensor_tensor(h[:, u % 2, j], act[:, u % 2, j], pair[(pairs[u] + j) % 2][1][:],
                                        ALU.mult).then_inc(pair_done, 1)

            def residual(u):
                layer, c = UNITS[u]
                ve.wait_ge(back_ready, u + 1)
                if layer == SSM:
                    ve.wait_ge(plus_ready, c + 1)
                dst, res = {FFN1: (x_ffn, x_in), SSM: (x_ssm, x_plus), FFN2: (x_out, x_ssm)}[layer]
                nc.vector.tensor_tensor(dst[:, c].rearrange("p t d -> p (t d)"), back[:],
                                        res[:, c].rearrange("p t d -> p (t d)"), ALU.add).then_inc(rows_ready, 1)

            nc.vector.memset(warm[:], 0.0).then_inc(const_ready, 1)
            prep(0)
            ve.wait_ge(gu_loaded, 32)
            nc.vector.tensor_copy(gu_raw[:], gu_int[:]).then_inc(gu_cast, 1)
            ve.wait_ge(weights_turned, 1)
            ve.wait_ge(weights_hi, 1)
            nc.vector.tensor_tensor(gu_lo[:, 0].rearrange("p j h -> p (j h)"), pair[0][0][:, 0:H],
                                    gu_hi[:, 0].rearrange("p j h -> p (j h)").bitcast(F32), ALU.subtract)
            nc.vector.tensor_tensor(gu_lo[:, 1].rearrange("p j h -> p (j h)"), pair[0][1][:, 0:H],
                                    gu_hi[:, 1].rearrange("p j h -> p (j h)").bitcast(F32),
                                    ALU.subtract).then_inc(pair_done, 1)
            turn(0)
            ve.wait_ge(down_loaded, 16)
            nc.vector.tensor_copy(close_raw[:, 0:J], down_int[:]).then_inc(down_cast, 1)
            prep(1)
            ve.wait_ge(vecs_loaded, 48)
            nc.vector.tensor_scalar(half_ab[:], vecs[:, 1:2], 0.5, None, ALU.mult)
            ve.wait_ge(weights_turned, 2)
            nc.vector.tensor_scalar(proj_scaled[:].rearrange("p n h -> p (n h)"), pair[1][1][:], vecs[:, 0:1], None,
                                    ALU.mult).then_inc(scaled_ready, 1)
            ve.wait_ge(weights_hi, 2)
            nc.vector.tensor_tensor(close_lo[:].rearrange("p j h -> p (j h)"), pair[1][0][:],
                                    close_hi[:].rearrange("p j h -> p (j h)").bitcast(F32),
                                    ALU.subtract).then_inc(pair_done, 1)
            ve.wait_ge(weights_hi, 3)
            nc.vector.tensor_tensor(proj_lo[:], proj_scaled[:], proj_hi[:].bitcast(F32),
                                    ALU.subtract).then_inc(weights_lo, 1)

            for k in range(NU + 2):
                if k < NU and is_ssm(k):
                    c, g = UNITS[k][1], pairs[k]
                    b = c % 2
                    ve.wait_ge(tanh_ready, 3 * c + 1)
                    ve.wait_ge(proj_ready, 4 * c + 2)
                    nc.vector.scalar_tensor_tensor(drive[:, b], tanh_d[:, b], 1.0, pair[g % 2][1][:], ALU.add,
                                                   ALU.mult).then_inc(pair_done, 1)
                    ve.wait_ge(tanh_ready, 3 * c + 2)
                    then_wait(nc.vector.tensor_scalar(decay[:, b], tanh_a[:, b], 0.5, 0.5, ALU.mult, ALU.add))
                    if k - 2 >= 0:
                        residual(k - 2)
                    ve.wait_ge(tanh_ready, 3 * c + 3)
                    ve.wait_ge(pair_done, g + 1)
                    start = state[:, c - B, T - 1:T] if c >= B else 0.0
                    nc.vector.tensor_tensor_scan(state[:, c], decay[:, b], drive[:, b], start, ALU.mult,
                                                 ALU.add).then_inc(pair_done, 1)
                    if k + 1 < NU:
                        turn(k + 1)
                    ve.wait_ge(pair_done, g + 2)
                    nc.vector.scalar_tensor_tensor(h[:, k % 2, 0], tanh_c[:, b], 1.0, state[:, c], ALU.add,
                                                   ALU.mult).then_inc(gated_ready, 1)
                    for u in preps_in(k):
                        prep(u)
                else:
                    if k < NU:
                        gate_times_up(k, 0)
                    if k - 2 >= 0:
                        residual(k - 2)
                    if k < NU:
                        gate_times_up(k, 1)
                    for u in preps_in(k):
                        prep(u)
                    if k < NU:
                        gate_times_up(k, 2)
                    if k + 1 < NU:
                        turn(k + 1)

        @block.tensor
        def _(pe):
            def product(dst, w_hi, w_lo, m_hi, m_lo, first=True, last=True):
                nc.tensor.matmul(dst, w_hi, m_hi, start=first, stop=False)
                nc.tensor.matmul(dst, w_hi, m_lo, start=False, stop=False)
                return nc.tensor.matmul(dst, w_lo, m_hi, start=False, stop=last)

            def turn(u):
                pe.wait_ge(normed_ready, u + 1)
                if u:
                    pe.wait_ge(xlo_ready, u)
                for t in range(R):
                    last = nc.tensor.transpose(turned[:, t * P:(t + 1) * P], normed[:, u % 4, t], ident[:])
                last.then_inc(turned_ready, 1)

            def close(u):
                if u:
                    pe.wait_ge(closed_ready, u)
                if is_ssm(u):
                    pe.wait_ge(hlo_ready, parts[u] + 1)
                    pe.wait_ge(hhi_ready, parts[u] + 1)
                    product(acc[:], close_hi[:, J], close_lo[:, J], hhi[:, u % 2, 0],
                            hlo[:, u % 2, 0]).then_inc(acc_ready, 1)
                    return
                for j in range(J):
                    pe.wait_ge(hhi_ready, parts[u] + j + 1)
                    pe.wait_ge(hlo_ready, parts[u] + j + 1)
                    last = product(acc[:], close_hi[:, j], close_lo[:, j], hhi[:, u % 2, j], hlo[:, u % 2, j],
                                   first=(j == 0), last=(j == J - 1))
                last.then_inc(acc_ready, 1)

            def turn_back(u):
                pe.wait_ge(closed_ready, u + 1)
                if u:
                    pe.wait_ge(rows_ready, u)
                for t in range(R):
                    last = nc.tensor.transpose(back[:, t * P:(t + 1) * P], closed[:, u % 2, t * P:(t + 1) * P], ident[:])
                last.then_inc(back_ready, 1)

            def gate_and_up(u, j):
                g = pairs[u] + j
                pe.wait_ge(pair_done, g - 1)
                for n, done in ((0, gate_ready), (1, up_ready)):
                    product(pair[g % 2][n][:], gu_hi[:, n, j], gu_lo[:, n, j], xhi[:, u % 2],
                            xlo[:, u % 2]).then_inc(done, 1)

            def projections(u, p):
                g = pairs[u] + p
                pe.wait_ge(pair_done, g - 1)
                for n in range(2):
                    product(pair[g % 2][n][:], proj_hi[:, 2 * p + n], proj_lo[:, 2 * p + n], xhi[:, u % 2],
                            xlo[:, u % 2]).then_inc(proj_ready, 1)

            pe.wait_ge(ident_ready, 1)
            pe.wait_ge(gu_cast, 1)
            for n in range(2):
                for j in range(J):
                    last = nc.tensor.transpose(pair[0][n][:, j * P:(j + 1) * P], gu_raw[:, n, j], ident[:])
            last.then_inc(weights_turned, 1)
            turn(0)
            pe.wait_ge(down_cast, 1)
            pe.wait_ge(ssm_loaded, 5 * 16)
            for j in range(J + 1):
                nc.tensor.transpose(pair[1][0][:, j * P:(j + 1) * P], close_raw[:, j], ident[:])
            for n in range(4):
                last = nc.tensor.transpose(pair[1][1][:, n * P:(n + 1) * P], proj_raw[:, n], ident[:])
            last.then_inc(weights_turned, 1)

            for k in range(NU + 2):
                if k < NU:
                    pe.wait_ge(xhi_ready, k + 1)
                    pe.wait_ge(xlo_ready, k + 1)
                    if is_ssm(k):
                        pe.wait_ge(weights_lo, 1)
                        projections(k, 0)
                    else:
                        gate_and_up(k, 0)
                if k - 2 >= 0:
                    turn_back(k - 2)
                if k < NU:
                    if is_ssm(k):
                        projections(k, 1)
                    else:
                        for j in range(1, J):
                            gate_and_up(k, j)
                if k + 1 < NU:
                    turn(k + 1)
                if 0 <= k - 1 < NU:
                    close(k - 1)


_INS = ['L0_attn_x', 'L0_attn_norm_w', 'L0_attn_A_w', 'L0_attn_A_b', 'L0_attn_B_w', 'L0_attn_C_w', 'L0_attn_D_w',
        'L0_attn_out_w', 'L0_attn_out_b', 'L0_ffn_w_gate', 'L0_ffn_w_up', 'L0_ffn_w_down']


def kernel(**inputs):
    import numpy as _np
    import concourse.bacc as _bacc
    from concourse import mybir as _mybir
    from concourse.bass_utils import run_bass_kernel_spmd as _run

    nc = _bacc.Bacc("TRN2", target_bir_lowering=False, num_devices=1)
    arrays, args = {}, []
    for name in _INS:
        a = _np.ascontiguousarray(inputs[name])
        arrays[f"in_{name}_dram"] = a
        args.append(nc.dram_tensor(f"in_{name}_dram", a.shape, _mybir.dt.from_np(a.dtype), kind="ExternalInput").ap())
    shape = inputs['L0_attn_x'].shape
    args.append(nc.dram_tensor("out_0_dram", shape, F32, kind="ExternalOutput").ap())
    macaron_kernel(nc, *args)
    r = _run(nc, [arrays], core_ids=[0])
    return r.results[0]["out_0_dram"]
```

```python
from contextlib import ExitStack

import concourse.bass as bass
from concourse import mybir

F32 = mybir.dt.float32
F32R = mybir.dt.float32r
I32 = mybir.dt.int32
ALU = mybir.AluOpType
ACT = mybir.ActivationFunctionType

P = 128
EPS = 1e-05
SCALE = 1.0 / 127.0
FFN1, SSM, FFN2 = 1, 2, 3

UNITS = [(FFN1, 0), (FFN1, 1), (FFN1, 2), (SSM, 0), (FFN1, 3), (SSM, 1), (SSM, 2), (FFN2, 0), (SSM, 3), (FFN2,
         1), (FFN2, 2), (FFN2, 3)]
NU = len(UNITS)

GPSIMD = """
    coefs:0.0 coefs:1.0 coefs:2.0 coefs:3.0 plus:3.0 coefs:4.0 coefs:5.0 plus:5.0 coefs:6.0 plus:6.0
    coefs:7.0 coefs:8.0 plus:8.0 coefs:9.0 coefs:10.0 coefs:11.0
"""
SCALAR = """
    norm:0.0 wcopy:0.0 xhi:0.0 norm:1.0 wcopy:1.0 silu:0.0 wcopy:2.0 norm:2.0 silu:0.1 silu:0.2 xhi:1.0
    closed:0.0 silu:1.0 silu:1.1 silu:1.2 xhi:2.0 closed:1.0 norm:3.0 silu:2.0 xhi:3.0 silu:2.1 norm:4.0
    silu:2.2 xhi:4.0 tanh:3.0 tanh:3.1 norm:5.0 tanh:3.2 closed:2.0 silu:4.0 xhi:5.0 silu:4.1 closed:3.0
    silu:4.2 norm:6.0 tanh:5.0 tanh:5.1 tanh:5.2 xhi:6.0 norm:7.0 closed:4.0 xhi:7.0 tanh:6.0 tanh:6.1
    tanh:6.2 closed:5.0 silu:7.0 norm:8.0 silu:7.1 closed:6.0 xhi:8.0 silu:7.2 norm:9.0 tanh:8.0 tanh:8.1
    tanh:8.2 xhi:9.0 norm:10.0 closed:7.0 silu:9.0 xhi:10.0 closed:8.0 silu:9.1 silu:9.2 silu:10.0 norm:11.0
    silu:10.1 silu:10.2 xhi:11.0 closed:9.0 silu:11.0 closed:10.0 silu:11.1 silu:11.2 closed:11.0
"""
VECTOR = """
    stats:0.0 wcast:0.0 stats:1.0 norm:0.0 wcast:1.0 wlow:0.0 norm:1.0 xlo:0.0 stats:2.0 wscale:0.0 mul:0.0
    norm:2.0 wlow:1.0 mul:0.1 mul:0.2 xlo:1.0 mul:1.0 mul:1.1 resid:0.0 stats:3.0 mul:1.2 xlo:2.0 stats:4.0
    norm:3.0 resid:1.0 mul:2.0 xlo:3.0 norm:4.0 mul:2.1 stats:5.0 mul:2.2 xlo:4.0 drive:3.0 norm:5.0
    decay:3.0 scan:3.0 gated:3.0 mul:4.0 resid:2.0 stats:6.0 xlo:5.0 mul:4.1 mul:4.2 resid:3.0 norm:6.0
    stats:7.0 decay:5.0 drive:5.0 xlo:6.0 norm:7.0 scan:5.0 gated:5.0 xlo:7.0 drive:6.0 resid:4.0 stats:8.0
    decay:6.0 scan:6.0 mul:7.0 gated:6.0 norm:8.0 resid:5.0 mul:7.1 stats:9.0 xlo:8.0 mul:7.2 resid:6.0
    norm:9.0 stats:10.0 drive:8.0 decay:8.0 xlo:9.0 scan:8.0 norm:10.0 gated:8.0 resid:7.0 mul:9.0 xlo:10.0
    mul:9.1 resid:8.0 stats:11.0 mul:9.2 mul:10.0 norm:11.0 mul:10.1 mul:10.2 xlo:11.0 mul:11.0 mul:11.1
    mul:11.2 resid:9.0 resid:10.0 resid:11.0
"""
TENSOR = """
    wturn:0.0 turn:0.0 wturn:1.0 main:0.0 main:0.1 main:0.2 turn:1.0 close:0.0 close:0.1 close:0.2 main:1.0
    main:1.1 back:0.0 main:1.2 turn:2.0 close:1.0 close:1.1 close:1.2 main:2.0 back:1.0 turn:3.0 main:2.1
    main:2.2 turn:4.0 main:3.0 close:2.0 main:3.1 close:2.1 close:2.2 main:4.0 back:2.0 turn:5.0 main:4.1
    close:3.0 main:4.2 back:3.0 main:5.0 main:5.1 turn:6.0 close:4.0 close:4.1 close:4.2 turn:7.0 main:6.0
    back:4.0 main:6.1 close:5.0 main:7.0 back:5.0 main:7.1 close:6.0 turn:8.0 main:7.2 back:6.0 close:7.0
    main:8.0 main:8.1 turn:9.0 close:7.1 close:7.2 main:9.0 back:7.0 turn:10.0 close:8.0 main:9.1 back:8.0
    close:9.0 main:9.2 main:10.0 main:10.1 main:10.2 turn:11.0 close:9.1 close:9.2 main:11.0 close:10.0
    close:10.1 close:10.2 main:11.1 main:11.2 back:9.0 close:11.0 close:11.1 close:11.2 back:10.0 back:11.0
"""


def steps(text):
    for word in text.split():
        step, place = word.split(":")
        yield step, *map(int, place.split("."))


def is_ssm(u):
    return UNITS[u][0] == SSM


def macaron_kernel(nc, x, norm_w, A_w, A_b, B_w, C_w, D_w, out_w, out_b, w_gate, w_up, w_down, out):
    B, L, D = x.shape
    H = w_gate.shape[0]
    J = H // P
    NC = 4
    T = B * L // NC
    R = T // P
    HALVES = NC // B
    assert D == P and H == J * P and T == 512 and A_w.shape == (P, P)

    def rows(ap, chunk):
        seq, half = chunk % B, chunk // B
        return ap[seq, half * T:(half + 1) * T, :].rearrange("(t p) d -> p t d", p=P)

    pairs = [1 + sum(2 if is_ssm(v) else J for v in range(u)) for u in range(NU)]
    ffns = [sum(not is_ssm(v) for v in range(u)) for u in range(NU)]

    with ExitStack() as ctx:
        def sb(name, shape, dt=F32):
            return ctx.enter_context(nc.sbuf_tensor(name, shape, dt))

        def ps(name):
            return ctx.enter_context(nc.psum_tensor(name, [P, 512], F32))

        def sem(name):
            return ctx.enter_context(nc.semaphore(name))

        x_in = sb("x_in", [P, NC, R, D])
        x_ffn = sb("x_ffn", [P, NC, R, D])
        x_plus = sb("x_plus", [P, NC, R, D])
        x_ssm = sb("x_ssm", [P, NC, R, D])
        x_out = sb("x_out", [P, NC, R, D])
        ident = sb("ident", [P, P])
        bn = sb("bn", [P, NU, R, 6])
        meanvar = sb("meanvar", [P, NU, R, 2])
        negmean = sb("negmean", [P, NU, R])
        pow_in = sb("pow_in", [P, NU, 2 * R])
        rstd = sb("rstd", [P, NU, 2 * R])
        rstd1 = sb("rstd1", [P, NC, R])
        shift = sb("shift", [P, NU, 2 * R])
        half_power = sb("half_power", [P, 2 * R])
        normed = sb("normed", [P, 4, R, D])
        xhi = sb("xhi", [P, 2, T], F32R)
        xlo = sb("xlo", [P, 2, T], F32R)
        act = sb("act", [P, 2, J, T])
        h = sb("h", [P, 2, J, T])
        tanh_d = sb("tanh_d", [P, 2, T])
        tanh_a = sb("tanh_a", [P, 2, T])
        tanh_c = sb("tanh_c", [P, 2, T])
        decay = sb("decay", [P, 2, T])
        drive = sb("drive", [P, 2, T])
        state = sb("state", [P, NC, T])
        closed = sb("closed", [P, 2, T])
        gu_int = sb("gu_int", [P, 2, J, P], I32)
        gu_raw = sb("gu_raw", [P, 2, J, P])
        gu_hi = sb("gu_hi", [P, 2, J, P], F32R)
        gu_lo = sb("gu_lo", [P, 2, J, P], F32R)
        down_int = sb("down_int", [P, J, P], I32)
        close_raw = sb("close_raw", [P, J + 1, P])
        close_w = sb("close_w", [P, J + 1, P])
        proj_raw = sb("proj_raw", [P, 4, P])
        proj_scaled = sb("proj_scaled", [P, 4, P])
        proj_hi = sb("proj_hi", [P, 4, P], F32R)
        proj_lo = sb("proj_lo", [P, 4, P], F32R)
        vecs = sb("vecs", [P, 3])
        half_ab = sb("half_ab", [P, 1])
        warm = sb("warm", [P, 1])

        pair = [[ps("pair0a"), ps("pair0b")], [ps("pair1a"), ps("pair1b")]]
        turned = ps("turned")
        acc = ps("acc")
        back = ps("back")

        x_loaded = [sem(f"x_loaded{c}") for c in range(NC)]
        gu_loaded = sem("gu_loaded")
        down_loaded = sem("down_loaded")
        ssm_loaded = sem("ssm_loaded")
        vecs_loaded = sem("vecs_loaded")
        x_stored = sem("x_stored")
        ident_ready = sem("ident_ready")
        const_ready = sem("const_ready")
        vec_own = sem("vec_own")
        pool_own = sem("pool_own")
        gu_cast = sem("gu_cast")
        down_cast = sem("down_cast")
        gu_turned = sem("gu_turned")
        gu_hi_ready = sem("gu_hi_ready")
        close_turned = sem("close_turned")
        close_w_ready = sem("close_w_ready")
        proj_turned = sem("proj_turned")
        scaled_ready = sem("scaled_ready")
        proj_hi_ready = sem("proj_hi_ready")
        proj_lo_ready = sem("proj_lo_ready")
        stats_ready = sem("stats_ready")
        coef_ready = sem("coef_ready")
        normed_v_ready = sem("normed_v_ready")
        normed_s_ready = sem("normed_s_ready")
        plus_ready = sem("plus_ready")
        turned_ready = sem("turned_ready")
        xhi_ready = sem("xhi_ready")
        xlo_ready = sem("xlo_ready")
        gate_ready = sem("gate_ready")
        up_ready = sem("up_ready")
        silu_ready = sem("silu_ready")
        pair_done = sem("pair_done")
        proj_ready = sem("proj_ready")
        tanh_ready = sem("tanh_ready")
        half_ab_ready = sem("half_ab_ready")
        decay_ready = sem("decay_ready")
        gated_ready = sem("gated_ready")
        acc_ready = sem("acc_ready")
        closed_ready = sem("closed_ready")
        back_ready = sem("back_ready")
        rows_ready = sem("rows_ready")

        def source(u):
            layer, c = UNITS[u]
            return {FFN1: x_in, SSM: x_ffn, FFN2: x_ssm}[layer][:, c]

        block = ctx.enter_context(nc.Block())

        @block.sync
        def _(sp):
            sp.dma_start(x_in[:, 0], rows(x, 0)).then_inc(x_loaded[0], 16)
            sp.dma_start(gu_int[:, 0], w_gate.rearrange("(j p) d -> p j d", p=P)).then_inc(gu_loaded, 16)
            sp.dma_start(gu_int[:, 1], w_up.rearrange("(j p) d -> p j d", p=P)).then_inc(gu_loaded, 16)
            sp.dma_start(x_in[:, 1], rows(x, 1)).then_inc(x_loaded[1], 16)
            for c in range(2, NC):
                sp.dma_start(x_in[:, c], rows(x, c)).then_inc(x_loaded[c], 16)
            for u in range(NU):
                layer, c = UNITS[u]
                if layer == FFN2:
                    sp.wait_ge(rows_ready, u + 1)
                    sp.dma_start(rows(out, c), x_out[:, c]).then_inc(x_stored, 16)
            sp.wait_ge(x_stored, 16 * NC)

        @block.gpsimd
        def _(pool):
            own = [0]

            def then_wait(ins):
                own[0] += 1
                ins.then_inc(pool_own, 1)
                pool.wait_ge(pool_own, own[0])

            then_wait(nc.gpsimd.memset(ident[:], 0.0))
            nc.gpsimd.affine_select(out=ident[:], in_=ident[:], compare_op=ALU.not_equal, fill=1.0, base=0,
                                    pattern=[[-1, P]], channel_multiplier=1).then_inc(ident_ready, 1)
            then_wait(nc.gpsimd.memset(half_power[:], -0.5))

            def coefs(u):
                layer = UNITS[u][0]
                pool.wait_ge(stats_ready, u + 1)
                n = 2 * R if layer == SSM else R
                then_wait(nc.gpsimd.tensor_tensor(rstd[:, u, 0:n], pow_in[:, u, 0:n], half_power[:, 0:n], ALU.pow))
                for i in range(n // R):
                    last = nc.gpsimd.tensor_tensor(shift[:, u, i * R:(i + 1) * R], negmean[:, u],
                                                   rstd[:, u, i * R:(i + 1) * R], ALU.mult)
                last.then_inc(coef_ready, 1)

            def plus(u):
                c = UNITS[u][1]
                then_wait(nc.gpsimd.tensor_scalar(rstd1[:, c], rstd[:, u, 0:R], 1.0, 1.0, ALU.mult, ALU.add))
                for t in range(R):
                    last = nc.gpsimd.tensor_scalar(x_plus[:, c, t], source(u)[:, t], rstd1[:, c, t:t + 1],
                                                   shift[:, u, t:t + 1], ALU.mult, ALU.add)
                last.then_inc(plus_ready, 1)

            for step, u, _ in steps(GPSIMD):
                if step == "coefs":
                    coefs(u)
                else:
                    plus(u)

        @block.scalar
        def _(sc):
            sc.wait_ge(const_ready, 1)
            nc.scalar.activation(warm[:], warm[:], ACT.Silu)
            sc.dma_start(down_int[:], w_down.rearrange("d (j h) -> d j h", h=P)).then_inc(down_loaded, 16)
            sc.dma_start(close_raw[:, J], out_w).then_inc(ssm_loaded, 16)
            for n, w in enumerate((D_w, B_w, A_w, C_w)):
                sc.dma_start(proj_raw[:, n], w).then_inc(ssm_loaded, 16)
            for n, v in enumerate((norm_w, A_b, out_b)):
                sc.dma_start(vecs[:, n:n + 1], v.rearrange("(p o) -> p o", o=1)).then_inc(vecs_loaded, 16)

            def weights(n):
                if n == 0:
                    sc.wait_ge(gu_turned, 1)
                    for i in range(2):
                        last = nc.scalar.activation(gu_hi[:, i].rearrange("p j h -> p (j h)"), pair[0][i][:, 0:H],
                                                    ACT.Copy)
                    last.then_inc(gu_hi_ready, 1)
                elif n == 1:
                    sc.wait_ge(close_turned, 1)
                    nc.scalar.activation(close_w[:].rearrange("p j h -> p (j h)"), acc[:],
                                         ACT.Copy).then_inc(close_w_ready, 1)
                else:
                    sc.wait_ge(scaled_ready, 1)
                    nc.scalar.activation(proj_hi[:], proj_scaled[:], ACT.Copy).then_inc(proj_hi_ready, 1)

            def normalise(u):
                s0 = R if is_ssm(u) else 0
                sc.wait_ge(coef_ready, u + 1)
                if u >= 4:
                    sc.wait_ge(turned_ready, u - 3)
                for t in range(R // 2, R):
                    last = nc.scalar.activation(normed[:, u % 4, t], source(u)[:, t], ACT.Identity,
                                                bias=shift[:, u, s0 + t:s0 + t + 1], scale=rstd[:, u, s0 + t:s0 + t + 1])
                last.then_inc(normed_s_ready, 1)

            def high_part(u):
                sc.wait_ge(turned_ready, u + 1)
                nc.scalar.activation(xhi[:, u % 2], turned[:], ACT.Copy).then_inc(xhi_ready, 1)

            def silu(u, j):
                g = pairs[u] + j
                sc.wait_ge(gate_ready, ffns[u] * J + j + 1)
                nc.scalar.activation(act[:, u % 2, j], pair[g % 2][0][:], ACT.Silu, scale=SCALE).then_inc(silu_ready, 1)

            def tanh(u, n):
                g, c = pairs[u], UNITS[u][1]
                bank = (pair[g % 2][0], pair[(g + 1) % 2][0], pair[(g + 1) % 2][1])[n]
                dst = (tanh_d, tanh_a, tanh_c)[n]
                sc.wait_ge(proj_ready, 4 * c + (1, 3, 4)[n])
                if n == 1:
                    sc.wait_ge(half_ab_ready, 1)
                nc.scalar.activation(dst[:, c % 2], bank[:], ACT.Tanh, scale=0.5,
                                     bias=half_ab[:] if n == 1 else 0.0).then_inc(tanh_ready, 1)

            def closed_columns(u):
                sc.wait_ge(acc_ready, u + 1)
                if is_ssm(u):
                    nc.scalar.activation(closed[:, u % 2], acc[:], ACT.Identity, scale=0.25,
                                         bias=vecs[:, 2:3]).then_inc(closed_ready, 1)
                else:
                    nc.scalar.activation(closed[:, u % 2], acc[:], ACT.Copy,
                                         scale=0.5 * SCALE * SCALE).then_inc(closed_ready, 1)

            for step, u, j in steps(SCALAR):
                if step == "wcopy":
                    weights(u)
                elif step == "norm":
                    normalise(u)
                elif step == "xhi":
                    high_part(u)
                elif step == "silu":
                    silu(u, j)
                elif step == "tanh":
                    tanh(u, j)
                else:
                    closed_columns(u)

        @block.vector
        def _(ve):
            own = [0]

            def then_wait(ins):
                own[0] += 1
                ins.then_inc(vec_own, 1)
                ve.wait_ge(vec_own, own[0])

            def stats(u):
                layer, c = UNITS[u]
                if layer == FFN1:
                    ve.wait_ge(x_loaded[c], 16)
                else:
                    ve.wait_ge(rows_ready, UNITS.index((layer - 1, c)) + 1)
                for t in range(R):
                    last = nc.vector.bn_stats(bn[:, u, t], source(u)[:, t])
                then_wait(last)
                for t in range(R):
                    last = nc.vector.bn_aggr(meanvar[:, u, t], bn[:, u, t])
                then_wait(last)
                nc.vector.tensor_scalar(negmean[:, u], meanvar[:, u, :, 0], -1.0, None, ALU.mult)
                if layer == SSM:
                    nc.vector.tensor_scalar(pow_in[:, u, R:2 * R], meanvar[:, u, :, 1], 1.0 + EPS, EPS * EPS,
                                            ALU.mult, ALU.add)
                nc.vector.tensor_scalar(pow_in[:, u, 0:R], meanvar[:, u, :, 1], EPS, None,
                                        ALU.add).then_inc(stats_ready, 1)

            def normalise(u):
                s0 = R if is_ssm(u) else 0
                ve.wait_ge(coef_ready, u + 1)
                if u >= 4:
                    ve.wait_ge(turned_ready, u - 3)
                for t in range(R // 2):
                    last = nc.vector.tensor_scalar(normed[:, u % 4, t], source(u)[:, t], negmean[:, u, t:t + 1],
                                                   rstd[:, u, s0 + t:s0 + t + 1], ALU.add, ALU.mult)
                last.then_inc(normed_v_ready, 1)

            def low_part(u):
                ve.wait_ge(turned_ready, u + 1)
                ve.wait_ge(xhi_ready, u + 1)
                nc.vector.tensor_tensor(xlo[:, u % 2], turned[:], xhi[:, u % 2].bitcast(F32),
                                        ALU.subtract).then_inc(xlo_ready, 1)

            def gate_times_up(u, j):
                ve.wait_ge(silu_ready, ffns[u] * J + j + 1)
                ve.wait_ge(up_ready, ffns[u] * J + j + 1)
                nc.vector.tensor_tensor(h[:, u % 2, j], act[:, u % 2, j], pair[(pairs[u] + j) % 2][1][:],
                                        ALU.mult).then_inc(pair_done, 1)

            def residual(u):
                layer, c = UNITS[u]
                ve.wait_ge(back_ready, u + 1)
                if layer == SSM:
                    ve.wait_ge(plus_ready, c + 1)
                dst, res = {FFN1: (x_ffn, x_in), SSM: (x_ssm, x_plus), FFN2: (x_out, x_ssm)}[layer]
                nc.vector.tensor_tensor(dst[:, c].rearrange("p t d -> p (t d)"), back[:],
                                        res[:, c].rearrange("p t d -> p (t d)"), ALU.add).then_inc(rows_ready, 1)

            def drive_of(u):
                c = UNITS[u][1]
                ve.wait_ge(tanh_ready, 3 * c + 1)
                ve.wait_ge(proj_ready, 4 * c + 2)
                nc.vector.scalar_tensor_tensor(drive[:, c % 2], tanh_d[:, c % 2], 1.0, pair[pairs[u] % 2][1][:],
                                               ALU.add, ALU.mult).then_inc(pair_done, 1)

            def decay_of(u):
                c = UNITS[u][1]
                ve.wait_ge(tanh_ready, 3 * c + 2)
                nc.vector.tensor_scalar(decay[:, c % 2], tanh_a[:, c % 2], 0.5, 0.5, ALU.mult,
                                        ALU.add).then_inc(decay_ready, 1)

            def scan(u):
                c = UNITS[u][1]
                ve.wait_ge(tanh_ready, 3 * c + 3)
                ve.wait_ge(pair_done, pairs[u] + 1)
                ve.wait_ge(decay_ready, c + 1)
                if c >= B:
                    ve.wait_ge(pair_done, pairs[UNITS.index((SSM, c - B))] + 2)
                start = state[:, c - B, T - 1:T] if c >= B else 0.0
                nc.vector.tensor_tensor_scan(state[:, c], decay[:, c % 2], drive[:, c % 2], start, ALU.mult,
                                             ALU.add).then_inc(pair_done, 1)

            def gated(u):
                c = UNITS[u][1]
                ve.wait_ge(pair_done, pairs[u] + 2)
                nc.vector.scalar_tensor_tensor(h[:, u % 2, 0], tanh_c[:, c % 2], 1.0, state[:, c], ALU.add,
                                               ALU.mult).then_inc(gated_ready, 1)

            def casts(n):
                if n == 0:
                    ve.wait_ge(gu_loaded, 32)
                    nc.vector.tensor_copy(gu_raw[:], gu_int[:]).then_inc(gu_cast, 1)
                else:
                    ve.wait_ge(down_loaded, 16)
                    nc.vector.tensor_copy(close_raw[:, 0:J], down_int[:]).then_inc(down_cast, 1)
                    ve.wait_ge(vecs_loaded, 48)
                    nc.vector.tensor_scalar(half_ab[:], vecs[:, 1:2], 0.5, None, ALU.mult).then_inc(half_ab_ready, 1)

            def scaled():
                ve.wait_ge(proj_turned, 1)
                ve.wait_ge(vecs_loaded, 48)
                nc.vector.tensor_scalar(proj_scaled[:].rearrange("p n h -> p (n h)"), back[:], vecs[:, 0:1], None,
                                        ALU.mult).then_inc(scaled_ready, 1)

            def weights_low(n):
                if n == 0:
                    ve.wait_ge(gu_turned, 1)
                    ve.wait_ge(gu_hi_ready, 1)
                    for i in range(2):
                        last = nc.vector.tensor_tensor(gu_lo[:, i].rearrange("p j h -> p (j h)"), pair[0][i][:, 0:H],
                                                       gu_hi[:, i].rearrange("p j h -> p (j h)").bitcast(F32),
                                                       ALU.subtract)
                    last.then_inc(pair_done, 1)
                else:
                    ve.wait_ge(proj_hi_ready, 1)
                    ve.wait_ge(scaled_ready, 1)
                    nc.vector.tensor_tensor(proj_lo[:], proj_scaled[:], proj_hi[:].bitcast(F32),
                                            ALU.subtract).then_inc(proj_lo_ready, 1)

            nc.vector.memset(warm[:], 0.0).then_inc(const_ready, 1)
            for step, u, j in steps(VECTOR):
                if step == "wcast":
                    casts(u)
                elif step == "wscale":
                    scaled()
                elif step == "wlow":
                    weights_low(u)
                elif step == "stats":
                    stats(u)
                elif step == "norm":
                    normalise(u)
                elif step == "xlo":
                    low_part(u)
                elif step == "mul":
                    gate_times_up(u, j)
                elif step == "drive":
                    drive_of(u)
                elif step == "decay":
                    decay_of(u)
                elif step == "scan":
                    scan(u)
                elif step == "gated":
                    gated(u)
                else:
                    residual(u)

        @block.tensor
        def _(pe):
            def product(dst, w_hi, w_lo, m_hi, m_lo, first=True, last=True):
                nc.tensor.matmul(dst, w_hi, m_hi, start=first, stop=False)
                nc.tensor.matmul(dst, w_hi, m_lo, start=False, stop=False)
                return nc.tensor.matmul(dst, w_lo, m_hi, start=False, stop=last)

            def turn(u):
                pe.wait_ge(normed_v_ready, u + 1)
                pe.wait_ge(normed_s_ready, u + 1)
                if u:
                    pe.wait_ge(xlo_ready, u)
                for t in range(R):
                    last = nc.tensor.transpose(turned[:, t * P:(t + 1) * P], normed[:, u % 4, t], ident[:])
                last.then_inc(turned_ready, 1)

            def close(u, j):
                if j == 0:
                    if u:
                        pe.wait_ge(closed_ready, u)
                    else:
                        pe.wait_ge(close_w_ready, 1)
                if is_ssm(u):
                    pe.wait_ge(gated_ready, UNITS[u][1] + 1)
                    nc.tensor.matmul(acc[:], close_w[:, J], h[:, u % 2, 0], start=True, stop=True).then_inc(acc_ready, 1)
                    return
                pe.wait_ge(pair_done, pairs[u] + j + 1)
                last = nc.tensor.matmul(acc[:], close_w[:, j], h[:, u % 2, j], start=(j == 0), stop=(j == J - 1))
                if j == J - 1:
                    last.then_inc(acc_ready, 1)

            def turn_back(u):
                pe.wait_ge(closed_ready, u + 1)
                if u:
                    pe.wait_ge(rows_ready, u)
                else:
                    pe.wait_ge(scaled_ready, 1)
                for t in range(R):
                    last = nc.tensor.transpose(back[:, t * P:(t + 1) * P], closed[:, u % 2, t * P:(t + 1) * P], ident[:])
                last.then_inc(back_ready, 1)

            def gate_and_up(u, j):
                g = pairs[u] + j
                pe.wait_ge(xhi_ready, u + 1)
                pe.wait_ge(xlo_ready, u + 1)
                pe.wait_ge(pair_done, max(g - 1, 1))
                for n, done in ((0, gate_ready), (1, up_ready)):
                    product(pair[g % 2][n][:], gu_hi[:, n, j], gu_lo[:, n, j], xhi[:, u % 2],
                            xlo[:, u % 2]).then_inc(done, 1)

            def projections(u, p):
                g = pairs[u] + p
                pe.wait_ge(xhi_ready, u + 1)
                pe.wait_ge(xlo_ready, u + 1)
                pe.wait_ge(proj_lo_ready, 1)
                pe.wait_ge(pair_done, g - 1)
                for n in range(2):
                    product(pair[g % 2][n][:], proj_hi[:, 2 * p + n], proj_lo[:, 2 * p + n], xhi[:, u % 2],
                            xlo[:, u % 2]).then_inc(proj_ready, 1)

            def weights(n):
                pe.wait_ge(ident_ready, 1)
                if n == 0:
                    pe.wait_ge(gu_cast, 1)
                    for i in range(2):
                        for j in range(J):
                            last = nc.tensor.transpose(pair[0][i][:, j * P:(j + 1) * P], gu_raw[:, i, j], ident[:])
                    last.then_inc(gu_turned, 1)
                    return
                pe.wait_ge(down_cast, 1)
                pe.wait_ge(ssm_loaded, 5 * 16)
                for j in range(J + 1):
                    last = nc.tensor.transpose(acc[:, j * P:(j + 1) * P], close_raw[:, j], ident[:])
                last.then_inc(close_turned, 1)
                for i in range(4):
                    last = nc.tensor.transpose(back[:, i * P:(i + 1) * P], proj_raw[:, i], ident[:])
                last.then_inc(proj_turned, 1)

            for step, u, j in steps(TENSOR):
                if step == "wturn":
                    weights(u)
                elif step == "turn":
                    turn(u)
                elif step == "main":
                    if is_ssm(u):
                        projections(u, j)
                    else:
                        gate_and_up(u, j)
                elif step == "close":
                    close(u, j)
                else:
                    turn_back(u)


_INS = ['L0_attn_x', 'L0_attn_norm_w', 'L0_attn_A_w', 'L0_attn_A_b', 'L0_attn_B_w', 'L0_attn_C_w', 'L0_attn_D_w',
        'L0_attn_out_w', 'L0_attn_out_b', 'L0_ffn_w_gate', 'L0_ffn_w_up', 'L0_ffn_w_down']


def kernel(**inputs):
    import numpy as _np
    import concourse.bacc as _bacc
    from concourse import mybir as _mybir
    from concourse.bass_utils import run_bass_kernel_spmd as _run

    nc = _bacc.Bacc("TRN2", target_bir_lowering=False, num_devices=1)
    arrays, args = {}, []
    for name in _INS:
        a = _np.ascontiguousarray(inputs[name])
        arrays[f"in_{name}_dram"] = a
        args.append(nc.dram_tensor(f"in_{name}_dram", a.shape, _mybir.dt.from_np(a.dtype), kind="ExternalInput").ap())
    shape = inputs['L0_attn_x'].shape
    args.append(nc.dram_tensor("out_0_dram", shape, F32, kind="ExternalOutput").ap())
    macaron_kernel(nc, *args)
    r = _run(nc, [arrays], core_ids=[0])
    return r.results[0]["out_0_dram"]
```

```python
from contextlib import ExitStack

import concourse.bass as bass
from concourse import mybir

F32 = mybir.dt.float32
F32R = mybir.dt.float32r
BF16 = mybir.dt.bfloat16
I32 = mybir.dt.int32
ALU = mybir.AluOpType
ACT = mybir.ActivationFunctionType

P = 128
EPS = 1e-05
SCALE = 1.0 / 127.0
FFN1, SSM, FFN2 = 1, 2, 3

UNITS = [(layer, chunk) for layer in (FFN1, SSM, FFN2) for chunk in range(4)]
NU = len(UNITS)
SPLIT_TILES = [0 if layer == SSM else 2 for layer, _ in UNITS]

GPSIMD = """
    coefs:0.0 norm:0.0 coefs:1.0 norm:1.0 coefs:2.0 norm:2.0 hlo:0.0 coefs:3.0 hlo:0.1 norm:3.0 hlo:1.0
    hlo:1.1 hlo:2.0 hlo:2.1 coefs:4.0 norm:4.0 plus:4.0 coefs:5.0 hlo:3.0 norm:5.0 hlo:3.1 decay:4.0
    plus:5.0 coefs:6.0 decay:5.0 norm:6.0 coefs:7.0 plus:6.0 norm:7.0 coefs:8.0 decay:6.0 norm:8.0 plus:7.0
    coefs:9.0 decay:7.0 norm:9.0 hlo:8.0 hlo:8.1 coefs:10.0 norm:10.0 hlo:9.0 coefs:11.0 norm:11.0 hlo:9.1
    hlo:10.0 hlo:10.1 hlo:11.0 hlo:11.1
"""
SCALAR = """
    norm:0.0 wcopy:0.0 xhi:0.0 norm:1.0 wcopy:1.0 silu:0.0 wcopy:2.0 silu:0.1 xhi:1.0 wsquare:0.0 norm:2.0
    hhi:0.0 silu:0.2 xhi:2.0 hhi:0.1 silu:1.0 norm:3.0 silu:1.1 hhi:1.0 silu:1.2 hhi:1.1 closed:0.0 silu:2.0
    silu:2.1 hhi:2.0 hhi:2.1 xhi:3.0 closed:1.0 silu:2.2 norm:4.0 closed:2.0 silu:3.0 silu:3.1 xhi:4.0
    hhi:3.0 silu:3.2 hhi:3.1 tanh:4.0 norm:5.0 tanh:4.1 tanh:4.2 xhi:5.0 closed:3.0 tanh:5.0 tanh:5.1
    tanh:5.2 norm:6.0 closed:4.0 xhi:6.0 norm:7.0 closed:5.0 tanh:6.0 tanh:6.1 tanh:6.2 xhi:7.0 norm:8.0
    tanh:7.0 xhi:8.0 tanh:7.1 tanh:7.2 norm:9.0 silu:8.0 closed:6.0 xhi:9.0 hhi:8.0 silu:8.1 silu:8.2
    hhi:8.1 closed:7.0 silu:9.0 hhi:9.0 norm:10.0 closed:8.0 silu:9.1 xhi:10.0 silu:9.2 hhi:9.1 norm:11.0
    silu:10.0 silu:10.1 hhi:10.0 xhi:11.0 hhi:10.1 silu:10.2 closed:9.0 silu:11.0 silu:11.1 hhi:11.0
    hhi:11.1 closed:10.0 silu:11.2 closed:11.0
"""
VECTOR = """
    stats:0.0 wcast:0.0 stats:1.0 wcast:1.0 wlow:0.0 xlo:0.0 wscale:0.0 stats:2.0 wlow:1.0 wlow:2.0 mul:0.0
    xlo:1.0 stats:3.0 wflag:0.0 mul:0.1 mul:0.2 xlo:2.0 mul:1.0 mul:1.1 mul:1.2 mul:2.0 mul:2.1 resid:0.0
    stats:4.0 xlo:3.0 mul:2.2 resid:1.0 stats:5.0 mul:3.0 mul:3.1 xlo:4.0 resid:2.0 mul:3.2 stats:6.0
    drive:4.0 xlo:5.0 scan:4.0 gated:4.0 drive:5.0 resid:3.0 stats:7.0 scan:5.0 gated:5.0 resid:4.0 xlo:6.0
    stats:8.0 drive:6.0 resid:5.0 stats:9.0 xlo:7.0 scan:6.0 gated:6.0 drive:7.0 xlo:8.0 scan:7.0 mul:8.0
    gated:7.0 xlo:9.0 resid:6.0 mul:8.1 stats:10.0 mul:8.2 mul:9.0 resid:7.0 stats:11.0 mul:9.1 xlo:10.0
    mul:9.2 resid:8.0 mul:10.0 mul:10.1 xlo:11.0 mul:10.2 mul:11.0 mul:11.1 resid:9.0 mul:11.2 resid:10.0
    resid:11.0
"""
TENSOR_HEAD = """
    wturn:0.0 turn:0.0 wturn:1.0 main:0.0 main:0.1 turn:1.0 main:0.2 wsum:0.0 turn:2.0
"""
TENSOR_REST = """
    main:1.0 main:1.1 close:0.0 main:1.2 close:0.1 close:0.2 main:2.0 main:2.1 back:0.0 close:1.0 close:1.1
    turn:3.0 close:1.2 main:2.2 back:1.0 close:2.0 close:2.1 close:2.2 main:3.0 main:3.1 turn:4.0 back:2.0
    main:3.2 main:4.0 main:4.1 close:3.0 turn:5.0 close:3.1 close:3.2 main:5.0 back:3.0 main:5.1 close:4.0
    turn:6.0 back:4.0 close:5.0 main:6.0 back:5.0 main:6.1 turn:7.0 main:7.0 turn:8.0 main:7.1 close:6.0
    main:8.0 turn:9.0 main:8.1 back:6.0 main:8.2 close:7.0 main:9.0 close:8.0 back:7.0 close:8.1 close:8.2
    main:9.1 turn:10.0 main:9.2 close:9.0 back:8.0 main:10.0 main:10.1 turn:11.0 close:9.1 main:10.2
    close:9.2 main:11.0 main:11.1 close:10.0 close:10.1 close:10.2 back:9.0 main:11.2 close:11.0 back:10.0
    close:11.1 close:11.2 back:11.0
"""


def steps(text):
    for word in text.split():
        step, place = word.split(":")
        yield step, *map(int, place.split("."))


def is_ssm(u):
    return UNITS[u][0] == SSM


def macaron_kernel(nc, x, norm_w, A_w, A_b, B_w, C_w, D_w, out_w, out_b, w_gate, w_up, w_down, out):
    B, L, D = x.shape
    H = w_gate.shape[0]
    J = H // P
    NC = 4
    IDLE_PRODUCTS = 11
    POOL_TILES = 2
    T = B * L // NC
    R = T // P
    HALVES = NC // B
    assert D == P and H == J * P and T == 512 and A_w.shape == (P, P)

    def rows(ap, chunk):
        seq, half = chunk % B, chunk // B
        return ap[seq, half * T:(half + 1) * T, :].rearrange("(t p) d -> p t d", p=P)

    pairs = [1 + sum(2 if is_ssm(v) else J for v in range(u)) for u in range(NU)]
    S = max(SPLIT_TILES)
    splits = [sum(SPLIT_TILES[:u]) for u in range(NU)]
    ffns = [sum(not is_ssm(v) for v in range(u)) for u in range(NU)]

    with ExitStack() as ctx:
        def sb(name, shape, dt=F32):
            return ctx.enter_context(nc.sbuf_tensor(name, shape, dt))

        def ps(name):
            return ctx.enter_context(nc.psum_tensor(name, [P, 512], F32))

        def sem(name):
            return ctx.enter_context(nc.semaphore(name))

        x_in = sb("x_in", [P, NC, R, D])
        x_ffn = sb("x_ffn", [P, NC, R, D])
        x_plus = sb("x_plus", [P, NC, R, D])
        x_ssm = sb("x_ssm", [P, NC, R, D])
        x_out = sb("x_out", [P, NC, R, D])
        ident = sb("ident", [P, P])
        bn = sb("bn", [P, NU, R, 6])
        meanvar = sb("meanvar", [P, NU, R, 2])
        negmean = sb("negmean", [P, NU, R])
        pow_in = sb("pow_in", [P, NU, 2 * R])
        rstd = sb("rstd", [P, NU, 2 * R])
        rstd1 = sb("rstd1", [P, NC, R])
        shift = sb("shift", [P, NU, 2 * R])
        half_power = sb("half_power", [P, 2 * R])
        normed = sb("normed", [P, 4, R, D])
        xhi = sb("xhi", [P, 2, T], F32R)
        xlo = sb("xlo", [P, 2, T], F32R)
        act = sb("act", [P, 2, J, T])
        h = sb("h", [P, 2, J, T])
        hhi = sb("hhi", [P, 2, S, T], F32R)
        hlo = sb("hlo", [P, 2, S, T], F32R)
        tanh_d = sb("tanh_d", [P, 2, T])
        tanh_a = sb("tanh_a", [P, 2, T])
        tanh_c = sb("tanh_c", [P, 2, T])
        decay = sb("decay", [P, 2, T])
        drive = sb("drive", [P, 2, T])
        state = sb("state", [P, NC, T])
        closed = sb("closed", [P, 2, T])
        gu_int = sb("gu_int", [P, 2, J, P], I32)
        gu_raw = sb("gu_raw", [P, 2, J, P])
        gu_hi = sb("gu_hi", [P, 2, J, P], F32R)
        ffn_lo = sb("ffn_lo", [P, 2 * J + S, P], F32R)
        gu_lo = ffn_lo[:, 0:2 * J].rearrange("p (i j) h -> p i j h", i=2)
        down_lo = ffn_lo[:, 2 * J:]
        down_hi = sb("down_hi", [P, S, P], F32R)
        down_int = sb("down_int", [P, J, P], I32)
        close_raw = sb("close_raw", [P, J + 1, P])
        close_w = sb("close_w", [P, J + 1, P])
        proj_raw = sb("proj_raw", [P, 4, P])
        proj_scaled = sb("proj_scaled", [P, 4, P])
        proj_hi = sb("proj_hi", [P, 4, P], F32R)
        proj_lo = sb("proj_lo", [P, 4, P], F32R)
        vecs = sb("vecs", [P, 3])
        half_ab = sb("half_ab", [P, 1])
        warm = sb("warm", [P, 1])
        idle_work = sb("idle_work", [P, T], BF16)
        ones = sb("ones", [P, 1])
        low_squares = sb("low_squares", [P, (2 * J + S) * P])
        low_sums = sb("low_sums", [P, 1])
        low_flag = sb("low_flag", [1, 1], I32)

        pair = [[ps("pair0a"), ps("pair0b")], [ps("pair1a"), ps("pair1b")]]
        turned = ps("turned")
        acc = ps("acc")
        back = ps("back")
        low_total = ps("low_total")

        def closing_parts(u):
            return [(acc, 0, T // 2), (low_total, T // 2, T // 2)] if u == NU - 1 else [(acc, 0, T)]

        x_loaded = [sem(f"x_loaded{c}") for c in range(NC)]
        gu_loaded = sem("gu_loaded")
        down_loaded = sem("down_loaded")
        ssm_loaded = sem("ssm_loaded")
        vecs_loaded = sem("vecs_loaded")
        x_stored = sem("x_stored")
        ident_ready = sem("ident_ready")
        ones_ready = sem("ones_ready")
        idle_ready = sem("idle_ready")
        const_ready = sem("const_ready")
        vec_own = sem("vec_own")
        pool_own = sem("pool_own")
        gu_cast = sem("gu_cast")
        down_cast = sem("down_cast")
        gu_turned = sem("gu_turned")
        gu_hi_ready = sem("gu_hi_ready")
        low_sums_ready = sem("low_sums_ready")
        low_total_ready = sem("low_total_ready")
        low_flag_ready = sem("low_flag_ready")
        close_turned = sem("close_turned")
        close_w_ready = sem("close_w_ready")
        down_lo_ready = sem("down_lo_ready")
        proj_turned = sem("proj_turned")
        scaled_ready = sem("scaled_ready")
        proj_hi_ready = sem("proj_hi_ready")
        proj_lo_ready = sem("proj_lo_ready")
        stats_ready = sem("stats_ready")
        coef_ready = sem("coef_ready")
        normed_g_ready = sem("normed_g_ready")
        normed_s_ready = sem("normed_s_ready")
        plus_ready = sem("plus_ready")
        turned_ready = sem("turned_ready")
        xhi_ready = sem("xhi_ready")
        xlo_ready = sem("xlo_ready")
        gate_ready = sem("gate_ready")
        up_ready = sem("up_ready")
        silu_ready = sem("silu_ready")
        last_h_ready = sem("last_h_ready")
        pair_done = sem("pair_done")
        proj_ready = sem("proj_ready")
        tanh_ready = sem("tanh_ready")
        half_ab_ready = sem("half_ab_ready")
        decay_ready = sem("decay_ready")
        gated_ready = sem("gated_ready")
        hhi_ready = sem("hhi_ready")
        hlo_ready = sem("hlo_ready")
        acc_ready = sem("acc_ready")
        closed_ready = sem("closed_ready")
        back_ready = sem("back_ready")
        rows_ready = sem("rows_ready")

        def source(u):
            layer, c = UNITS[u]
            return {FFN1: x_in, SSM: x_ffn, FFN2: x_ssm}[layer][:, c]

        block = ctx.enter_context(nc.Block())

        @block.sync
        def _(sp):
            sp.dma_start(x_in[:, 0], rows(x, 0)).then_inc(x_loaded[0], 16)
            sp.dma_start(gu_int[:, 0], w_gate.rearrange("(j p) d -> p j d", p=P)).then_inc(gu_loaded, 16)
            sp.dma_start(gu_int[:, 1], w_up.rearrange("(j p) d -> p j d", p=P)).then_inc(gu_loaded, 16)
            sp.dma_start(x_in[:, 1], rows(x, 1)).then_inc(x_loaded[1], 16)
            sp.dma_start(down_int[:], w_down.rearrange("d (j h) -> d j h", h=P)).then_inc(down_loaded, 16)
            sp.dma_start(close_raw[:, J], out_w).then_inc(ssm_loaded, 16)
            for n, w in enumerate((D_w, B_w, A_w, C_w)):
                sp.dma_start(proj_raw[:, n], w).then_inc(ssm_loaded, 16)
            for c in range(2, NC):
                sp.dma_start(x_in[:, c], rows(x, c)).then_inc(x_loaded[c], 16)
            for u in range(NU):
                layer, c = UNITS[u]
                if layer == FFN2 and u < NU - 1:
                    sp.wait_ge(rows_ready, u + 1)
                    sp.dma_start(rows(out, c), x_out[:, c]).then_inc(x_stored, 16)
            c = UNITS[NU - 1][1]
            for t in range(0, R, R // 2):
                sp.wait_ge(rows_ready, NU + (1 if t else 0))
                sp.dma_start(rows(out, c)[:, t:t + R // 2], x_out[:, c, t:t + R // 2]).then_inc(x_stored, 16)
            sp.wait_ge(x_stored, 16 * (NC + 1))

        @block.gpsimd
        def _(pool):
            own = [0]

            def then_wait(ins):
                own[0] += 1
                ins.then_inc(pool_own, 1)
                pool.wait_ge(pool_own, own[0])

            then_wait(nc.gpsimd.memset(ident[:], 0.0))
            nc.gpsimd.affine_select(out=ident[:], in_=ident[:], compare_op=ALU.not_equal, fill=1.0, base=0,
                                    pattern=[[-1, P]], channel_multiplier=1).then_inc(ident_ready, 1)
            for n, v in enumerate((norm_w, A_b, out_b)):
                pool.dma_start(vecs[:, n:n + 1], v.rearrange("(p o) -> p o", o=1)).then_inc(vecs_loaded, 16)
            nc.gpsimd.memset(ones[:], 1.0).then_inc(ones_ready, 1)
            then_wait(nc.gpsimd.memset(half_power[:], -0.5))

            def coefs(u):
                layer = UNITS[u][0]
                pool.wait_ge(stats_ready, u + 1)
                n = 2 * R if layer == SSM else R
                then_wait(nc.gpsimd.tensor_tensor(rstd[:, u, 0:n], pow_in[:, u, 0:n], half_power[:, 0:n], ALU.pow))
                for i in range(n // R):
                    last = nc.gpsimd.tensor_tensor(shift[:, u, i * R:(i + 1) * R], negmean[:, u],
                                                   rstd[:, u, i * R:(i + 1) * R], ALU.mult)
                last.then_inc(coef_ready, 1)

            def plus(u):
                c = UNITS[u][1]
                then_wait(nc.gpsimd.tensor_scalar(rstd1[:, c], rstd[:, u, 0:R], 1.0, 1.0, ALU.mult, ALU.add))
                for t in range(R):
                    last = nc.gpsimd.tensor_scalar(x_plus[:, c, t], source(u)[:, t], rstd1[:, c, t:t + 1],
                                                   shift[:, u, t:t + 1], ALU.mult, ALU.add)
                last.then_inc(plus_ready, 1)

            def normalise(u):
                s0 = R if is_ssm(u) else 0
                if u >= 4:
                    pool.wait_ge(turned_ready, u - 3)
                for t in range(POOL_TILES):
                    last = nc.gpsimd.tensor_scalar(normed[:, u % 4, t], source(u)[:, t], negmean[:, u, t:t + 1],
                                                   rstd[:, u, s0 + t:s0 + t + 1], ALU.add, ALU.mult)
                last.then_inc(normed_g_ready, 1)

            def low_part(u, j):
                pool.wait_ge(hhi_ready, splits[u] + j + 1)
                nc.gpsimd.tensor_tensor(hlo[:, u % 2, j], h[:, u % 2, j], hhi[:, u % 2, j].bitcast(F32),
                                        ALU.subtract).then_inc(hlo_ready, 1)

            def decay_of(u):
                c = UNITS[u][1]
                pool.wait_ge(tanh_ready, 3 * c + 2)
                nc.gpsimd.tensor_scalar(decay[:, c % 2], tanh_a[:, c % 2], 0.5, 0.5, ALU.mult,
                                        ALU.add).then_inc(decay_ready, 1)

            for step, u, j in steps(GPSIMD):
                if step == "coefs":
                    coefs(u)
                elif step == "norm":
                    normalise(u)
                elif step == "decay":
                    decay_of(u)
                elif step == "hlo":
                    low_part(u, j)
                else:
                    plus(u)

        @block.scalar
        def _(sc):
            sc.wait_ge(const_ready, 1)
            nc.scalar.activation(warm[:], warm[:], ACT.Silu)

            def weights(n):
                if n == 0:
                    sc.wait_ge(gu_turned, 1)
                    for i in range(2):
                        last = nc.scalar.activation(gu_hi[:, i].rearrange("p j h -> p (j h)"), pair[0][i][:, 0:H],
                                                    ACT.Copy)
                    last.then_inc(gu_hi_ready, 1)
                elif n == 1:
                    sc.wait_ge(close_turned, 1)
                    nc.scalar.activation(close_w[:, 1:].rearrange("p j h -> p (j h)"), acc[:, P:],
                                         ACT.Copy).then_inc(close_w_ready, 1)
                    nc.scalar.activation(down_hi[:].rearrange("p j h -> p (j h)"), acc[:, 0:S * P],
                                         ACT.Copy).then_inc(close_w_ready, 1)
                else:
                    sc.wait_ge(scaled_ready, 1)
                    nc.scalar.activation(proj_hi[:], proj_scaled[:], ACT.Copy).then_inc(proj_hi_ready, 1)

            def low_squared():
                sc.wait_ge(pair_done, 1)
                sc.wait_ge(down_lo_ready, 1)
                nc.scalar.activation(low_squares[:], ffn_lo[:].rearrange("p j h -> p (j h)").bitcast(F32),
                                     ACT.Square, accum_out=low_sums[:]).then_inc(low_sums_ready, 1)

            def normalise(u):
                s0 = R if is_ssm(u) else 0
                sc.wait_ge(coef_ready, u + 1)
                if u >= 4:
                    sc.wait_ge(turned_ready, u - 3)
                for t in range(POOL_TILES, R):
                    last = nc.scalar.activation(normed[:, u % 4, t], source(u)[:, t], ACT.Identity,
                                                bias=shift[:, u, s0 + t:s0 + t + 1], scale=rstd[:, u, s0 + t:s0 + t + 1])
                last.then_inc(normed_s_ready, 1)

            def high_part(u):
                sc.wait_ge(turned_ready, u + 1)
                nc.scalar.activation(xhi[:, u % 2], turned[:], ACT.Copy).then_inc(xhi_ready, 1)

            def silu(u, j):
                g = pairs[u] + j
                sc.wait_ge(gate_ready, ffns[u] * J + j + 1)
                nc.scalar.activation(act[:, u % 2, j], pair[g % 2][0][:], ACT.Silu, scale=SCALE).then_inc(silu_ready, 1)

            def h_high_part(u, j):
                sc.wait_ge(pair_done, pairs[u] + j + 1)
                nc.scalar.activation(hhi[:, u % 2, j], h[:, u % 2, j], ACT.Copy).then_inc(hhi_ready, 1)

            def tanh(u, n):
                g, c = pairs[u], UNITS[u][1]
                bank = (pair[g % 2][0], pair[(g + 1) % 2][0], pair[(g + 1) % 2][1])[n]
                dst = (tanh_d, tanh_a, tanh_c)[n]
                sc.wait_ge(proj_ready, 4 * c + (1, 3, 4)[n])
                if n == 1:
                    sc.wait_ge(half_ab_ready, 1)
                nc.scalar.activation(dst[:, c % 2], bank[:], ACT.Tanh, scale=0.5,
                                     bias=half_ab[:] if n == 1 else 0.0).then_inc(tanh_ready, 1)

            def closed_columns(u):
                sc.wait_ge(acc_ready, u + 1)
                if is_ssm(u):
                    nc.scalar.activation(closed[:, u % 2], acc[:], ACT.Identity, scale=0.25,
                                         bias=vecs[:, 2:3]).then_inc(closed_ready, 1)
                else:
                    for dst, i, n in closing_parts(u):
                        if i:
                            sc.wait_ge(acc_ready, u + 2)
                        nc.scalar.activation(closed[:, u % 2, i:i + n], dst[:, 0:n], ACT.Copy,
                                             scale=0.5 * SCALE * SCALE).then_inc(closed_ready, 1)

            for step, u, j in steps(SCALAR):
                if step == "wcopy":
                    weights(u)
                elif step == "wsquare":
                    low_squared()
                elif step == "norm":
                    normalise(u)
                elif step == "xhi":
                    high_part(u)
                elif step == "silu":
                    silu(u, j)
                elif step == "hhi":
                    h_high_part(u, j)
                elif step == "tanh":
                    tanh(u, j)
                else:
                    closed_columns(u)

        @block.vector
        def _(ve):
            own = [0]

            def then_wait(ins):
                own[0] += 1
                ins.then_inc(vec_own, 1)
                ve.wait_ge(vec_own, own[0])

            def stats(u):
                layer, c = UNITS[u]
                if layer != FFN1:
                    ve.wait_ge(rows_ready, UNITS.index((layer - 1, c)) + 1)
                else:
                    ve.wait_ge(x_loaded[c], 16)
                for t in range(R):
                    last = nc.vector.bn_stats(bn[:, u, t], source(u)[:, t])
                then_wait(last)
                for t in range(R):
                    last = nc.vector.bn_aggr(meanvar[:, u, t], bn[:, u, t])
                then_wait(last)
                nc.vector.tensor_scalar(negmean[:, u], meanvar[:, u, :, 0], -1.0, None, ALU.mult)
                if layer == SSM:
                    nc.vector.tensor_scalar(pow_in[:, u, R:2 * R], meanvar[:, u, :, 1], 1.0 + EPS, EPS * EPS,
                                            ALU.mult, ALU.add)
                nc.vector.tensor_scalar(pow_in[:, u, 0:R], meanvar[:, u, :, 1], EPS, None,
                                        ALU.add).then_inc(stats_ready, 1)

            def low_part(u):
                ve.wait_ge(turned_ready, u + 1)
                ve.wait_ge(xhi_ready, u + 1)
                nc.vector.tensor_tensor(xlo[:, u % 2], turned[:], xhi[:, u % 2].bitcast(F32),
                                        ALU.subtract).then_inc(xlo_ready, 1)

            def gate_times_up(u, j):
                ve.wait_ge(silu_ready, ffns[u] * J + j + 1)
                ve.wait_ge(up_ready, ffns[u] * J + j + 1)
                if u == NU - 1 and j == J - 1:
                    for i in (0, T // 2):
                        nc.vector.tensor_tensor(h[:, u % 2, j, i:i + T // 2], act[:, u % 2, j, i:i + T // 2],
                                                pair[(pairs[u] + j) % 2][1][:, i:i + T // 2],
                                                ALU.mult).then_inc(last_h_ready, 1)
                    return
                nc.vector.tensor_tensor(h[:, u % 2, j], act[:, u % 2, j], pair[(pairs[u] + j) % 2][1][:],
                                        ALU.mult).then_inc(pair_done, 1)

            def residual(u):
                layer, c = UNITS[u]
                ve.wait_ge(back_ready, u + 1)
                if layer == SSM:
                    ve.wait_ge(plus_ready, c + 1)
                dst, res = {FFN1: (x_ffn, x_in), SSM: (x_ssm, x_plus), FFN2: (x_out, x_ssm)}[layer]
                n = R // 2 if u == NU - 1 else R
                for t in range(0, R, n):
                    if t:
                        ve.wait_ge(back_ready, u + 2)
                    nc.vector.tensor_tensor(dst[:, c, t:t + n].rearrange("p t d -> p (t d)"), (turned if t else back)[:, t * P:(t + n) * P],
                                            res[:, c, t:t + n].rearrange("p t d -> p (t d)"),
                                            ALU.add).then_inc(rows_ready, 1)

            def drive_of(u):
                c = UNITS[u][1]
                ve.wait_ge(tanh_ready, 3 * c + 1)
                ve.wait_ge(proj_ready, 4 * c + 2)
                nc.vector.scalar_tensor_tensor(drive[:, c % 2], tanh_d[:, c % 2], 1.0, pair[pairs[u] % 2][1][:],
                                               ALU.add, ALU.mult).then_inc(pair_done, 1)

            def scan(u):
                c = UNITS[u][1]
                ve.wait_ge(tanh_ready, 3 * c + 3)
                ve.wait_ge(pair_done, pairs[u] + 1)
                ve.wait_ge(decay_ready, c + 1)
                if c >= B:
                    ve.wait_ge(pair_done, pairs[UNITS.index((SSM, c - B))] + 2)
                start = state[:, c - B, T - 1:T] if c >= B else 0.0
                nc.vector.tensor_tensor_scan(state[:, c], decay[:, c % 2], drive[:, c % 2], start, ALU.mult,
                                             ALU.add).then_inc(pair_done, 1)

            def gated(u):
                c = UNITS[u][1]
                ve.wait_ge(pair_done, pairs[u] + 2)
                nc.vector.scalar_tensor_tensor(h[:, u % 2, 0], tanh_c[:, c % 2], 1.0, state[:, c], ALU.add,
                                               ALU.mult).then_inc(gated_ready, 1)

            def casts(n):
                if n == 0:
                    ve.wait_ge(gu_loaded, 32)
                    nc.vector.tensor_copy(gu_raw[:], gu_int[:]).then_inc(gu_cast, 1)
                else:
                    ve.wait_ge(down_loaded, 16)
                    nc.vector.tensor_copy(close_raw[:, 0:J], down_int[:]).then_inc(down_cast, 1)

            def flag():
                ve.wait_ge(low_total_ready, 1)
                nc.vector.tensor_scalar(low_flag[:], low_total[0:1, 0:1], 1.0, None, ALU.min).then_inc(low_flag_ready, 1)

            def scaled():
                ve.wait_ge(vecs_loaded, 48)
                nc.vector.tensor_scalar(half_ab[:], vecs[:, 1:2], 0.5, None, ALU.mult).then_inc(half_ab_ready, 1)
                ve.wait_ge(proj_turned, 1)
                nc.vector.tensor_scalar(proj_scaled[:].rearrange("p n h -> p (n h)"), back[:], vecs[:, 0:1], None,
                                        ALU.mult).then_inc(scaled_ready, 1)

            def weights_low(n):
                if n == 0:
                    ve.wait_ge(gu_turned, 1)
                    ve.wait_ge(gu_hi_ready, 1)
                    for i in range(2):
                        last = nc.vector.tensor_tensor(gu_lo[:, i].rearrange("p j h -> p (j h)"), pair[0][i][:, 0:H],
                                                       gu_hi[:, i].rearrange("p j h -> p (j h)").bitcast(F32),
                                                       ALU.subtract)
                    last.then_inc(pair_done, 1)
                elif n == 2:
                    ve.wait_ge(close_w_ready, 2)
                    nc.vector.tensor_tensor(down_lo.rearrange("p j h -> p (j h)"), acc[:, 0:S * P],
                                            down_hi[:].rearrange("p j h -> p (j h)").bitcast(F32),
                                            ALU.subtract).then_inc(down_lo_ready, 1)
                else:
                    ve.wait_ge(proj_hi_ready, 1)
                    ve.wait_ge(scaled_ready, 1)
                    nc.vector.tensor_tensor(proj_lo[:], proj_scaled[:], proj_hi[:].bitcast(F32),
                                            ALU.subtract).then_inc(proj_lo_ready, 1)

            nc.vector.memset(idle_work[:], 0.0).then_inc(idle_ready, 1)
            nc.vector.memset(warm[:], 0.0).then_inc(const_ready, 1)
            for step, u, j in steps(VECTOR):
                if step == "wcast":
                    casts(u)
                elif step == "wscale":
                    scaled()
                elif step == "wflag":
                    flag()
                elif step == "wlow":
                    weights_low(u)
                elif step == "stats":
                    stats(u)
                elif step == "xlo":
                    low_part(u)
                elif step == "mul":
                    gate_times_up(u, j)
                elif step == "drive":
                    drive_of(u)
                elif step == "scan":
                    scan(u)
                elif step == "gated":
                    gated(u)
                else:
                    residual(u)

        @block.tensor
        def _(pe):
            def product(dst, w_hi, w_lo, m_hi, m_lo, low_ready, opens=True, closes=True):
                nc.tensor.matmul(dst, w_hi, m_hi, start=opens, stop=False)
                if w_lo is not None:
                    nc.tensor.matmul(dst, w_lo, m_hi, start=False, stop=False)
                pe.wait_ge(*low_ready)
                return nc.tensor.matmul(dst, w_hi, m_lo, start=False, stop=closes)

            def turn(u):
                pe.wait_ge(normed_g_ready, u + 1)
                pe.wait_ge(normed_s_ready, u + 1)
                if u:
                    pe.wait_ge(xlo_ready, u)
                for t in range(R):
                    last = nc.tensor.transpose(turned[:, t * P:(t + 1) * P], normed[:, u % 4, t], ident[:])
                last.then_inc(turned_ready, 1)

            def close(u, j, low):
                if j == 0:
                    if u:
                        pe.wait_ge(closed_ready, u)
                    else:
                        pe.wait_ge(down_lo_ready, 1)
                        pe.wait_ge(close_w_ready, 2)
                if is_ssm(u):
                    pe.wait_ge(gated_ready, UNITS[u][1] + 1)
                    nc.tensor.matmul(acc[:], close_w[:, J], h[:, u % 2, 0], start=True, stop=True).then_inc(acc_ready, 1)
                    return
                if j < SPLIT_TILES[u]:
                    pe.wait_ge(hhi_ready, splits[u] + j + 1)
                    for dst, i, n in closing_parts(u):
                        product(dst[:, 0:n], down_hi[:, j], down_lo[:, j] if low else None, hhi[:, u % 2, j, i:i + n],
                                hlo[:, u % 2, j, i:i + n], (hlo_ready, splits[u] + j + 1), opens=(j == 0), closes=False)
                    return
                if u < NU - 1 or j < J - 1:
                    pe.wait_ge(pair_done, pairs[u] + j + 1)
                for k, (dst, i, n) in enumerate(closing_parts(u)):
                    if u == NU - 1 and j == J - 1:
                        pe.wait_ge(last_h_ready, k + 1)
                    last = nc.tensor.matmul(dst[:, 0:n], close_w[:, j], h[:, u % 2, j, i:i + n], start=False,
                                            stop=(j == J - 1))
                    if j == J - 1:
                        last.then_inc(acc_ready, 1)

            def turn_back(u):
                pe.wait_ge(closed_ready, u + 1)
                if u:
                    pe.wait_ge(rows_ready, u)
                else:
                    pe.wait_ge(scaled_ready, 1)
                n = R // 2 if u == NU - 1 else R
                for i in range(0, R, n):
                    if i:
                        pe.wait_ge(closed_ready, u + 2)
                    for t in range(i, i + n):
                        last = nc.tensor.transpose((turned if i else back)[:, t * P:(t + 1) * P],
                                                   closed[:, u % 2, t * P:(t + 1) * P], ident[:])
                    last.then_inc(back_ready, 1)

            def gate_and_up(u, j, low):
                g = pairs[u] + j
                pe.wait_ge(xhi_ready, u + 1)
                if g == 1:
                    pe.wait_ge(gu_hi_ready, 1)
                    for n in range(2):
                        nc.tensor.matmul(pair[1][n][:], gu_hi[:, n, 0], xhi[:, 0], start=True, stop=False)
                    pe.wait_ge(pair_done, 1)
                    for n, done in ((0, gate_ready), (1, up_ready)):
                        nc.tensor.matmul(pair[1][n][:], gu_lo[:, n, 0], xhi[:, 0], start=False, stop=False)
                        pe.wait_ge(xlo_ready, 1)
                        nc.tensor.matmul(pair[1][n][:], gu_hi[:, n, 0], xlo[:, 0], start=False,
                                         stop=True).then_inc(done, 1)
                    return
                pe.wait_ge(pair_done, g - 1)
                for n, done in ((0, gate_ready), (1, up_ready)):
                    product(pair[g % 2][n][:], gu_hi[:, n, j], gu_lo[:, n, j] if low else None, xhi[:, u % 2],
                            xlo[:, u % 2], (xlo_ready, u + 1)).then_inc(done, 1)

            def projections(u, p):
                g = pairs[u] + p
                pe.wait_ge(xhi_ready, u + 1)
                pe.wait_ge(proj_lo_ready, 1)
                pe.wait_ge(pair_done, g - 1)
                for n in range(2):
                    product(pair[g % 2][n][:], proj_hi[:, 2 * p + n], proj_lo[:, 2 * p + n], xhi[:, u % 2],
                            xlo[:, u % 2], (xlo_ready, u + 1)).then_inc(proj_ready, 1)

            def weights(n):
                pe.wait_ge(ident_ready, 1)
                if n == 0:
                    pe.wait_ge(gu_cast, 1)
                    for i in range(2):
                        for j in range(J):
                            last = nc.tensor.transpose(pair[0][i][:, j * P:(j + 1) * P], gu_raw[:, i, j], ident[:])
                    last.then_inc(gu_turned, 1)
                    return
                pe.wait_ge(down_cast, 1)
                pe.wait_ge(ssm_loaded, 5 * 16)
                for j in range(J + 1):
                    last = nc.tensor.transpose(acc[:, j * P:(j + 1) * P], close_raw[:, j], ident[:])
                last.then_inc(close_turned, 1)
                for i in range(4):
                    last = nc.tensor.transpose(back[:, i * P:(i + 1) * P], proj_raw[:, i], ident[:])
                last.then_inc(proj_turned, 1)

            def low_summed():
                pe.wait_ge(low_sums_ready, 1)
                pe.wait_ge(ones_ready, 1)
                nc.tensor.matmul(low_total[0:1, 0:1], low_sums[:], ones[:], start=True,
                                 stop=True).then_inc(low_total_ready, 1)

            def run(text, low):
                for step, u, j in steps(text):
                    if step == "wturn":
                        weights(u)
                    elif step == "wsum":
                        low_summed()
                    elif step == "turn":
                        turn(u)
                    elif step == "main":
                        if is_ssm(u):
                            projections(u, j)
                        else:
                            gate_and_up(u, j, low)
                    elif step == "close":
                        close(u, j, low)
                    else:
                        turn_back(u)

            pe.wait_ge(idle_ready, 1)
            for _ in range(IDLE_PRODUCTS):
                nc.tensor.matmul(low_total[:], idle_work[:, 0:P], idle_work[:], start=True, stop=True)
            run(TENSOR_HEAD, True)
            pe.wait_ge(low_flag_ready, 1)
            has_low = pe.value_load(low_flag[0:1, 0:1], min_val=0, max_val=1)
            with pe.If(has_low == 0):
                run(TENSOR_REST, False)
            with pe.Else():
                run(TENSOR_REST, True)


_INS = ['L0_attn_x', 'L0_attn_norm_w', 'L0_attn_A_w', 'L0_attn_A_b', 'L0_attn_B_w', 'L0_attn_C_w', 'L0_attn_D_w',
        'L0_attn_out_w', 'L0_attn_out_b', 'L0_ffn_w_gate', 'L0_ffn_w_up', 'L0_ffn_w_down']


def kernel(**inputs):
    import numpy as _np
    import concourse.bacc as _bacc
    from concourse import mybir as _mybir
    from concourse.bass_utils import run_bass_kernel_spmd as _run

    nc = _bacc.Bacc("TRN2", target_bir_lowering=False, num_devices=1)
    arrays, args = {}, []
    for name in _INS:
        a = _np.ascontiguousarray(inputs[name])
        arrays[f"in_{name}_dram"] = a
        args.append(nc.dram_tensor(f"in_{name}_dram", a.shape, _mybir.dt.from_np(a.dtype), kind="ExternalInput").ap())
    shape = inputs['L0_attn_x'].shape
    args.append(nc.dram_tensor("out_0_dram", shape, F32, kind="ExternalOutput").ap())
    macaron_kernel(nc, *args)
    r = _run(nc, [arrays], core_ids=[0])
    return r.results[0]["out_0_dram"]
```
